# Optimizing a Trainium2 kernel written in Bass

```python
import numpy as np
import jax
import jax.numpy as jnp

def _softmax(x, axis=-1):
    return jax.nn.softmax(x, axis=axis)
def _gelu(x):
    return jax.nn.gelu(x, approximate=True)
def _silu(x):
    return jax.nn.silu(x)
def _sigmoid(x):
    return jax.nn.sigmoid(x)
def _layernorm(x, axis=-1, eps=1e-5):
    m = jnp.mean(x, axis=axis, keepdims=True)
    v = jnp.var(x, axis=axis, keepdims=True)
    return (x - m) / jnp.sqrt(v + eps)
def _scatter_add(tgt, idx, src, axis=0):
    return tgt.at[idx].add(src)
def _segment_sum(src, seg, n):
    return jax.ops.segment_sum(src, seg, n)

kernel_name = 'mk_conv_preact_d1_conv_nhwc256_5d8b51'

def setup_inputs(seed: int = 0):
    np.random.seed(seed)
    _w = jnp.asarray
    def _rec_inputs():
        import jax
        import jax.numpy as jnp
        _gk = jax.random.key(seed)
        x = -0.0003929 + 0.9999 * jax.random.normal(jax.random.fold_in(_gk, 1), (2, 128, 256, 256), jnp.float32)
        return x
    x = _rec_inputs()
    def _L0_conv_setup():
        import jax, jax.numpy as jnp
        import numpy as np
        NUM_HEADS = 4
        key = jax.random.key(seed)
        ks = jax.random.split(key, 5)
        B, T, F, C = (2, 128, 256, 256)
        s = 1.0 / np.sqrt(C)
        return {'x': jax.random.normal(ks[0], (B, T, F, C), jnp.float32), 'w_in': jax.random.normal(ks[1], (3 * C, C), jnp.float32) * s, 'b_in': jax.random.normal(ks[2], (3 * C,), jnp.float32) * 0.01, 'w_out': jax.random.normal(ks[3], (C, C), jnp.float32) * s, 'b_out': jax.random.normal(ks[4], (C,), jnp.float32) * 0.01, 'band': 16}
    _L0_conv_all = _L0_conv_setup()
    _L0_conv_in = {k: v for k, v in _L0_conv_all.items() if k in ('w_in', 'b_in', 'w_out', 'b_out', )}
    del _L0_conv_all

    return {
        "x": x,
        "L0_conv_w_in": _L0_conv_in["w_in"],
        "L0_conv_b_in": _L0_conv_in["b_in"],
        "L0_conv_w_out": _L0_conv_in["w_out"],
        "L0_conv_b_out": _L0_conv_in["b_out"],
    }

def reference(x, L0_conv_w_in, L0_conv_b_in, L0_conv_w_out, L0_conv_b_out):
    import jax
    import jax.numpy as jnp
    def _L0_conv_ref(x, w_in, b_in, w_out, b_out, band):
        import jax, jax.numpy as jnp
        import numpy as np
        NUM_HEADS = 4
        B, T, F, C = x.shape
        H = NUM_HEADS
        D = C // H
        x2 = x.reshape(B * T, F, C)
        qkv = x2 @ w_in.T + b_in
        q, k, v = jnp.split(qkv, 3, axis=-1)

        def heads(t):
            return t.reshape(B * T, F, H, D).transpose(0, 2, 1, 3)
        q, k, v = (heads(q), heads(k), heads(v))
        scores = jnp.einsum('bhid,bhjd->bhij', q, k) / jnp.sqrt(jnp.asarray(D, x.dtype))
        i = jnp.arange(F)[:, None]
        j = jnp.arange(F)[None, :]
        keep = jnp.abs(i - j) <= band
        scores = jnp.where(keep, scores, -jnp.inf)
        attn = jax.nn.softmax(scores, axis=-1)
        out = jnp.einsum('bhij,bhjd->bhid', attn, v)
        out = out.transpose(0, 2, 1, 3).reshape(B * T, F, C)
        y = out @ w_out.T + b_out
        return y.reshape(B, T, F, C)

    def _gn(v, G=32, eps=1e-5):
        B_, H_, W_, C_ = v.shape
        g = v.reshape(B_, H_, W_, G, C_ // G)
        m = jnp.mean(g, axis=(1, 2, 4), keepdims=True)
        s = jnp.var(g, axis=(1, 2, 4), keepdims=True)
        return ((g - m) / jnp.sqrt(s + eps)).reshape(v.shape)

    def _ln_c(v, eps=1e-6):
        m = jnp.mean(v, axis=-1, keepdims=True)
        s = jnp.var(v, axis=-1, keepdims=True)
        return (v - m) / jnp.sqrt(s + eps)

    def _ln_t(v, eps=1e-5):
        m = jnp.mean(v, axis=-1, keepdims=True)
        s = jnp.var(v, axis=-1, keepdims=True)
        return (v - m) / jnp.sqrt(s + eps)

    def _to_tokens(v):
        B_, H_, W_, C_ = v.shape
        return v.reshape(B_, H_ * W_, C_)
    def _from_tokens(t, like):
        return t.reshape(like.shape)

    x = x + _L0_conv_ref(_gn(x), L0_conv_w_in, L0_conv_b_in, L0_conv_w_out, L0_conv_b_out, 16)
    return x


_drawn_inputs = setup_inputs


def setup_inputs(seed=0):
    import zlib

    import numpy as np

    out = dict(_drawn_inputs(seed))
    spreads = {}
    factors = {'L0_conv_b_in': 4.876, 'L0_conv_b_out': 6.043}
    for name, (base, spread) in spreads.items():
        noise = np.random.default_rng([zlib.crc32(name.encode()), seed]).standard_normal(out[name].shape)
        drawn = base * np.exp(spread * noise) if base else spread * noise
        out[name] = jnp.asarray(drawn.astype(out[name].dtype))
    for name, factor in factors.items():
        out[name] = (out[name] * factor).astype(out[name].dtype)
    return out
```

```python
from contextlib import ExitStack

import numpy as np

import concourse.bass as bass
from concourse import mybir
from concourse.alu_op_type import AluOpType as ALU

F32 = mybir.dt.float32
F32R = mybir.dt.float32r
ACT = mybir.ActivationFunctionType
AX_X = mybir.AxisListType.X

P = 128
HEADS = 4
BAND = 16
GROUPS = 32
EPS = 1e-5
MASKED = -1e30
QB = 32
KB = 64
XRING = 4
STAT_RING = 3
CHUNK = 4


def block_order(seq):
    wide = seq // KB
    even = [(KB * a + BAND, KB * a, 2 * a + 1) for a in range(wide)]
    odd = [((KB * a - BAND) % seq, (KB * a - QB) % seq, 2 * a) for a in range(wide)]
    return even + odd


def constants(seq):
    mask = np.full((P, seq // QB, KB), MASKED, np.float32)
    for blk, (q0, k0, _) in enumerate(block_order(seq)):
        q = (q0 + np.arange(QB)) % seq
        k = (k0 + np.arange(KB)) % seq
        keep = np.abs(q[:, None] - k[None, :]) <= BAND
        mask[:, blk][np.tile(keep, (HEADS, 1))] = 0.0
    unit = np.eye(P, dtype=np.float32)
    size = 2 * P // GROUPS
    average = np.kron(np.eye(P // size, dtype=np.float32), np.full((size, size), 1.0 / size, np.float32))
    return mask.reshape(P, -1), unit, average


class Row:

    def __init__(self, fixed, turn=None):
        self.fixed, self.turn = fixed, turn

    def __add__(self, n):
        return Row(self.fixed + n, self.turn)

    def __sub__(self, n):
        return self + -n

    def over(self, n):
        if self.turn is None:
            return self.fixed // n
        return self.turn * (XRING // n) + self.fixed // n

    def slot(self, n):
        return self.fixed % n

    def counts(self, per_row=1):
        return (self.over(1) + 1) * per_row


def banded_attention(nc, x, w_in_t, w_out_t, b_in_c, b_out_r, mask_d, unit_d, average_d, out):
    B, R, SEQ, C = x.shape
    D = C // HEADS
    E = D + 1
    KH = C // P
    TT = SEQ // P
    NB = SEQ // QB
    W3 = 3 * C
    ROWS = B * R
    QSCALE = float(D) ** -0.5
    assert (B, HEADS * QB, KH, TT, D, KB) == (2, P, 2, 2, 64, 2 * QB) and 2 * BAND == QB
    HALO = BAND
    BLOCKS = block_order(SEQ)

    FIRST_CHUNKS = R // CHUNK + 1
    assert FIRST_CHUNKS % STAT_RING == 0
    LOOP0, LOOP0_END = 2, R - 2
    LOOP1, LOOP1_END = R, ROWS - XRING
    assert (LOOP0_END - LOOP0) % XRING == 0 and (LOOP1_END - LOOP1) % XRING == 0
    assert (LOOP0_END - LOOP0) == R - CHUNK

    x_rows = x.rearrange("b r (t p) c -> p (b r) t c", p=P)
    out_rows = out.rearrange("b r (t p) c -> p (b r) t c", p=P)

    with ExitStack() as ctx:
        def sb(name, shape, dt=F32):
            return ctx.enter_context(nc.sbuf_tensor(name, shape, dt))

        def psum(name, shape):
            return ctx.enter_context(nc.psum_tensor(name, shape, F32))

        def sem(name):
            return ctx.enter_context(nc.semaphore(name))

        unit = sb("unit", [P, P])
        average = sb("average", [P, P])
        mask = sb("mask", [P, NB * KB])
        b_in = sb("b_in", [P, W3 // P])
        bq = sb("bq", [P, KH])
        b_out = sb("b_out", [P, C])
        w_in = sb("w_in", [P, KH, W3])
        w_out = sb("w_out", [P, KH, C])
        w_scaled = sb("w_scaled", [P, KH, W3])
        w_hi = [sb(f"w_hi{b}", [P, KH, W3], F32R) for b in range(B)]
        w_lo = [sb(f"w_lo{b}", [P, KH, W3], F32R) for b in range(B)]
        wo_hi = sb("wo_hi", [P, KH, C], F32R)
        wo_lo = sb("wo_lo", [P, KH, C], F32R)

        stat_x = sb("stat_x", [P, STAT_RING, CHUNK * TT, C])
        pair_x = sb("pair_x", [P, 2, 2 * TT, C])
        moments = sb("moments", [P, KH, ROWS // 2, 6])
        stat = sb("stat", [P, KH, 2])
        neg_mean = [sb(f"neg_mean{b}", [P, KH]) for b in range(B)]
        rstd = sb("rstd", [P, KH])
        t1 = sb("t1", [P, KH])
        t2 = sb("t2", [P, KH])

        xr = sb("xr", [P, XRING, TT, C])
        res = sb("res", [P, XRING, TT, C])
        xT = sb("xT", [P, 2, 2, KH, HALO + SEQ], F32R)
        q_sb = sb("q_sb", [P, KH, NB, 2, QB])
        k_sb = sb("k_sb", [P, KH, SEQ])
        v_even = sb("v_even", [P, 2, TT, HEADS, E])
        v_odd = sb("v_odd", [P, 2, TT, HEADS, E])
        score = sb("score", [P, NB, KB])
        peak = sb("peak", [P, NB])
        prob = sb("prob", [P, NB * KB])
        probT = sb("probT", [P, 4, HEADS, 2, QB])
        inv = sb("inv", [P, TT, HEADS])
        o_sb = sb("o_sb", [P, TT, C])
        oT = sb("oT", [P, 2, KH, SEQ + HALO], F32R)

        ps_x = psum("ps_x", [P, KH, SEQ])
        ps_qk = psum("ps_qk", [P, 4, SEQ])
        ps_v = psum("ps_v", [P, TT, C])
        ps_s = psum("ps_s", [P, NB, KB])
        ps_p = psum("ps_p", [P, 4, P])
        ps_o = psum("ps_o", [P, TT, 512])
        ps_oT = ps_o[:, 1, :].rearrange("p (k s) -> p k s", k=KH)
        ps_y = ps_s[:].rearrange("p a b -> p (a b)").rearrange("p (t c) -> p t c", t=TT)
        stat_banks = [ps_x[:].rearrange("p a b -> p (a b)"), ps_v[:].rearrange("p a b -> p (a b)"),
                      ps_qk[:, 0:2].rearrange("p a b -> p (a b)"), ps_qk[:, 2:4].rearrange("p a b -> p (a b)")]
        ps_x_flat = stat_banks[0]

        consts_in = sem("consts_in")
        stat_in = [sem(f"stat_in{i}") for i in range(STAT_RING)]
        stat_turned = sem("stat_turned")
        stat_taken = sem("stat_taken")
        pair_in = [sem(f"pair_in{i}") for i in range(2)]
        pair_turned = sem("pair_turned")
        pair_taken = sem("pair_taken")
        fin_dve = sem("fin_dve")
        fin_pe = sem("fin_pe")
        fin_act = sem("fin_act")
        ones_set = sem("ones_set")
        zeros_set = sem("zeros_set")
        bq_made = sem("bq_made")
        pe_idle = sem("pe_idle")
        pool_idle = sem("pool_idle")

        x_in = [sem(f"x_in{i}") for i in range(2)]
        x_turned = sem("x_turned")
        xhi_made = sem("xhi_made")
        xlo_made = sem("xlo_made")
        res_made = sem("res_made")
        qk_done = sem("qk_done")
        qk_kept = sem("qk_kept")
        x_wrapped = sem("x_wrapped")
        v_done = sem("v_done")
        v_kept = sem("v_kept")
        v_moved = [sem(f"v_moved{i}") for i in range(2)]
        s_done = sem("s_done")
        s_masked = sem("s_masked")
        peak_found = sem("peak_found")
        s_shifted = sem("s_shifted")
        exp_done = sem("exp_done")
        p_turned = sem("p_turned")
        p_kept = sem("p_kept")
        o_done = sem("o_done")
        inv_made = sem("inv_made")
        o_kept = sem("o_kept")
        o_turned = sem("o_turned")
        ohi_made = sem("ohi_made")
        olo_made = sem("olo_made")
        halo_made = sem("halo_made")
        y_done = sem("y_done")
        y_kept = sem("y_kept")
        y_out = [sem(f"y_out{i}") for i in range(XRING)]

        CONSTS = 7
        FD = 16
        QK_STEPS = 3 * KH

        block = ctx.enter_context(nc.Block())

        def main(eng, step):
            for t in range(LOOP0):
                step(Row(t), 0, None)
            with eng.Fori(0, (LOOP0_END - LOOP0) // XRING) as turn:
                for k in range(XRING):
                    step(Row(LOOP0 + k, turn), 0, Row(k, turn))
            for t in range(LOOP0_END, R):
                step(Row(t), 0, None)
            with eng.Fori(0, (LOOP1_END - LOOP1) // XRING) as turn:
                for k in range(XRING):
                    step(Row(LOOP1 + k, turn), 1, None)
            for t in range(LOOP1_END, ROWS):
                step(Row(t), 1, None)

        def stand_alone(eng, idle, row):
            if row.turn is not None:
                eng.sem_inc(idle, 1)

        def exists(row):
            return row.turn is not None or 0 <= row.fixed < ROWS

        def batch_of(row, b):
            return row.fixed // R if row.turn is None else b

        def later(row):
            return row.turn is not None or row.fixed >= 0

        @block.sync
        def _(sp):
            for dst, src in ((unit, unit_d), (average, average_d), (mask, mask_d), (b_in, b_in_c),
                             (b_out, b_out_r)):
                sp.dma_start(dst[:], src).then_inc(consts_in, 16)
            sp.dma_start(w_in[:], w_in_t.rearrange("(k p) n -> p k n", p=P)).then_inc(consts_in, 16)
            sp.dma_start(w_out[:], w_out_t.rearrange("(k p) n -> p k n", p=P)).then_inc(consts_in, 16)

            def load_stat(place, turn_no, wait):
                if wait is not None:
                    sp.wait_ge(stat_turned, wait)
                sp.dma_start(stat_x[:, place].rearrange("p (r t) c -> p r t c", t=TT),
                             x_rows[:, bass.ds(turn_no * CHUNK, CHUNK)]).then_inc(stat_in[place], 16)

            for n in range(STAT_RING):
                load_stat(n, n, None)
            with sp.Fori(0, FIRST_CHUNKS // STAT_RING - 1) as turn:
                for n in range(STAT_RING):
                    load_stat(n, turn * STAT_RING + STAT_RING + n, turn * (4 * STAT_RING) + 4 * (n + 1))

            def load_x(row):
                if row.turn is not None or row.fixed >= XRING:
                    sp.wait_ge(x_turned, (row - XRING + 1).counts())
                    sp.wait_ge(res_made, (row - XRING + 1).counts())
                at = row.slot(XRING)
                sp.dma_start(xr[:, at:at + 2], x_rows[:, bass.ds(row.over(1), 2)]).then_inc(
                    x_in[row.slot(XRING) // 2], 16)

            def load_pair(pair_row):
                if pair_row.turn is not None or pair_row.fixed >= XRING:
                    sp.wait_ge(pair_turned, (pair_row - XRING + 1).counts())
                at = pair_row.slot(XRING) // 2
                sp.dma_start(pair_x[:, at].rearrange("p (r t) c -> p r t c", t=TT),
                             x_rows[:, bass.ds(pair_row.over(1) * -1 + (ROWS - 2), 2)]).then_inc(pair_in[at], 16)

            load_x(Row(0))
            load_x(Row(2))
            load_pair(Row(0))
            load_pair(Row(2))

            def step(t, b, pair):
                if t.fixed % 2 == 0 and exists(t + XRING):
                    load_x(t + XRING)
                if exists(t - 1):
                    store(t - 1)
                if exists(t + 1):
                    move_v(t + 1)
                if pair is not None and pair.fixed % 2 == 1:
                    load_pair(pair + 3)

            def store(row):
                sp.wait_ge(y_kept, row.counts())
                at = row.slot(XRING)
                sp.dma_start(out_rows[:, bass.ds(row.over(1), 1)], res[:, at:at + 1]).then_inc(y_out[at], 16)

            def move_v(row):
                if row.turn is None and row.fixed == 0:
                    sp.wait_ge(ones_set, 1)
                sp.wait_ge(v_kept, row.counts())
                if later(row - 2):
                    sp.wait_ge(o_done, (row - 2).counts())
                h = row.slot(2)
                sp.dma_start(v_odd[QB:P, h], v_even[0:P - QB, h]).then_inc(v_moved[h], 16)
                sp.dma_start(v_odd[0:QB, h, 0], v_even[P - QB:P, h, TT - 1]).then_inc(v_moved[h], 16)
                sp.dma_start(v_odd[0:QB, h, 1], v_even[P - QB:P, h, 0]).then_inc(v_moved[h], 16)

            move_v(Row(0))
            main(sp, step)
            store(Row(ROWS - 1))
            for at in range(XRING):
                sp.wait_ge(y_out[at], 16 * (ROWS // XRING))

        @block.tensor
        def _(pe):
            def mm(o, l, r, start=True, stop=True):
                return pe.matmul(o, l, r, start=start, stop=stop)

            pe.wait_ge(consts_in, 16 * CONSTS)

            def turn_chunk(n, before):
                for bank in range(4):
                    k, u = bank // 2, bank % 2
                    if before is not None:
                        pe.wait_ge(stat_taken, before - 4 + bank + 1)
                    for j in range(4):
                        last = pe.transpose(stat_banks[bank][:, P * j:P * (j + 1)],
                                            stat_x[:, n, 4 * u + j, P * k:P * (k + 1)], unit[:])
                    last.then_inc(stat_turned, 1)

            for n in range(STAT_RING):
                pe.wait_ge(stat_in[n], 16)
                turn_chunk(n, 4 * n if n else None)
            with pe.Fori(0, FIRST_CHUNKS // STAT_RING - 1) as turn:
                for n in range(STAT_RING):
                    pe.wait_ge(stat_in[n], turn * 16 + 32)
                    turn_chunk(n, turn * (4 * STAT_RING) + 4 * (STAT_RING + n))

            def average_groups(b):
                pe.wait_ge(fin_dve, FD * b + 2)
                mm(ps_x_flat[:, 0:2 * KH], average[:], stat[:].rearrange("p a b -> p (a b)")).then_inc(fin_pe, 1)
                pe.wait_ge(fin_dve, FD * b + 5)
                mm(ps_x_flat[:, 8:8 + KH], average[:], t2[:]).then_inc(fin_pe, 1)

            def turn_x(row, pair=None):
                pe.wait_ge(x_in[row.slot(XRING) // 2], (row.over(XRING) + 1) * 16)
                if later(row - 1):
                    pe.wait_ge(xlo_made, (row - 1).counts(KH))
                if pair is not None:
                    pe.wait_ge(pair_taken, pair.counts())
                if row.turn is None and row.fixed % R == 0:
                    pe.wait_ge(fin_dve, FD * (row.fixed // R) + 7)
                for k in range(KH):
                    for t in range(TT):
                        last = pe.transpose(ps_x[:, k, P * t:P * (t + 1)],
                                            xr[:, row.slot(XRING), t, P * k:P * (k + 1)], unit[:])
                last.then_inc(x_turned, 1)

            def turn_pair(pair):
                pe.wait_ge(pair_in[pair.slot(XRING) // 2], (pair.over(XRING) + 1) * 16)
                k = pair.slot(2)
                for j in range(2 * TT):
                    last = pe.transpose(ps_x_flat[:, P * j:P * (j + 1)],
                                        pair_x[:, pair.slot(XRING) // 2, j, P * k:P * (k + 1)], unit[:])
                last.then_inc(pair_turned, 1)

            def three(o, l_hi, l_lo, r_hi, r_lo, k):
                mm(o, l_hi, r_hi, start=k == 0, stop=False)
                mm(o, l_hi, r_lo, start=False, stop=False)
                return mm(o, l_lo, r_hi, start=False, stop=k == KH - 1)

            def project_qk(row, b):
                h = row.slot(2)
                if row.turn is None and row.fixed % R == 0:
                    pe.wait_ge(fin_dve, FD * (b + 1))
                pe.wait_ge(xlo_made, row.counts(KH))
                for m in (2, 3, 0, 1):
                    if later(row - 1) and m % 2 == 0:
                        pe.wait_ge(qk_kept, (row - 1).over(1) * QK_STEPS + (KH if m else QK_STEPS))
                    if m == 0:
                        pe.wait_ge(x_wrapped, row.counts())
                    tokens = slice(HALO, HALO + SEQ) if m >= KH else slice(0, SEQ)
                    for k in range(KH):
                        cols = slice(P * m, P * (m + 1))
                        last = three(ps_qk[:, m], w_hi[b][:, k, cols], w_lo[b][:, k, cols],
                                     xT[:, h, 0, k, tokens], xT[:, h, 1, k, tokens], k)
                    last.then_inc(qk_done, 1)

            def project_v(row, b):
                h = row.slot(2)
                if later(row - 1):
                    pe.wait_ge(v_kept, (row - 1).counts())
                for t in range(TT):
                    cols = slice(HALO + P * t, HALO + P * (t + 1))
                    for k in range(KH):
                        last = three(ps_v[:, t], xT[:, h, 0, k, cols], xT[:, h, 1, k, cols],
                                     w_hi[b][:, k, 2 * C:], w_lo[b][:, k, 2 * C:], k)
                last.then_inc(v_done, 1)

            def window(ap, start, size):
                if start + size <= SEQ:
                    return ap[:, start:start + size]
                n = SEQ - start
                assert n * 2 == size
                return ap.rearrange("p (a b) -> p a b", b=n)[:, ::-(SEQ // n - 1)]

            def scores(row):
                pe.wait_ge(qk_kept, row.counts(QK_STEPS))
                if later(row - 1):
                    pe.wait_ge(s_masked, (row - 1).counts())
                if later(row - 2):
                    pe.wait_ge(y_kept, (row - 2).counts())
                stand_alone(pe, pe_idle, row)
                for blk, (_, k0, place) in enumerate(BLOCKS):
                    for two in range(KH):
                        last = mm(ps_s[2 * QB * two:2 * QB * (two + 1), blk],
                                  q_sb[:, two, place].rearrange("p a b -> p (a b)"),
                                  window(k_sb[:, two], k0, KB))
                last.then_inc(s_done, 1)

            def turn_p(row):
                pe.wait_ge(exp_done, row.counts())
                if later(row - 1):
                    pe.wait_ge(p_kept, (row - 1).counts(2))
                for i in range(4):
                    last = pe.transpose(ps_p[:, i], prob[:, P * i:P * (i + 1)], unit[:])
                last.then_inc(p_turned, 1)

            def weigh_v(row):
                half = row.slot(2)
                pe.wait_ge(p_kept, row.counts(2))
                pe.wait_ge(v_moved[half], (row.over(2) + 1) * 48)
                if later(row - 1):
                    pe.wait_ge(olo_made, (row - 1).counts(KH))
                stand_alone(pe, pe_idle, row)
                for i in range(4):
                    v = v_even if i < 2 else v_odd
                    rows = slice(2 * QB, P) if i < 2 else slice(0, 2 * QB)
                    for h in range(HEADS):
                        last = mm(ps_o[rows, i % 2, E * h:E * (h + 1)],
                                  probT[:, i, h].rearrange("p a b -> p (a b)"), v[:, half, i % 2, h])
                last.then_inc(o_done, 1)

            def turn_o(row):
                pe.wait_ge(o_kept, row.counts())
                for k in range(KH):
                    for t in range(TT):
                        o = ps_oT[:, k, P * t:P * (t + 1)].rearrange("p (c u q) -> p u c q", c=2, u=2)
                        last = pe.transpose(o, o_sb[:, t, P * k:P * (k + 1)], unit[:])
                last.then_inc(o_turned, 1)

            def project_out(row, after):
                pe.wait_ge(halo_made, row.counts())
                if exists(after):
                    pe.wait_ge(s_masked, after.counts())
                for t in range(TT):
                    cols = slice(HALO + P * t, HALO + P * (t + 1))
                    for k in range(KH):
                        last = three(ps_y[:, t], oT[:, 0, k, cols], oT[:, 1, k, cols],
                                     wo_hi[:, k], wo_lo[:, k], k)
                last.then_inc(y_done, 1)

            average_groups(0)
            turn_x(Row(0))
            project_qk(Row(0), 0)
            project_v(Row(0), 0)
            turn_x(Row(1))

            def step(t, b, pair):
                scores(t)
                if later(t - 1):
                    turn_o(t - 1)
                if exists(t + 1):
                    project_qk(t + 1, batch_of(t + 1, b))
                if pair is not None:
                    turn_pair(pair)
                if t.turn is None and t.fixed == LOOP0_END:
                    average_groups(1)
                if later(t - 1):
                    project_out(t - 1, t)
                turn_p(t)
                if exists(t + 2):
                    turn_x(t + 2, pair)
                if exists(t + 1):
                    project_v(t + 1, batch_of(t + 1, b))
                weigh_v(t)

            main(pe, step)
            turn_o(Row(ROWS - 1))
            project_out(Row(ROWS - 1), Row(ROWS))

        @block.scalar
        def _(act):
            def split_w(b):
                act.wait_ge(fin_dve, FD * b + 7)
                act.activation(rstd[:], t1[:], ACT.Sqrt).then_inc(fin_act, 1)
                for k in range(KH):
                    act.wait_ge(fin_dve, FD * b + 13 + k)
                    act.activation(w_hi[b][:, k], w_scaled[:, k], ACT.Identity).then_inc(fin_act, 1)

            def x_high(row, b):
                if row.turn is None and row.fixed % R == 0:
                    act.wait_ge(fin_dve, FD * b + 3)
                act.wait_ge(x_turned, row.counts())
                if later(row - 2):
                    act.wait_ge(v_done, (row - 2).counts())
                for k in range(KH):
                    act.activation(xT[:, row.slot(2), 0, k, HALO:], ps_x[:, k], ACT.Identity,
                                   bias=neg_mean[b][:, k:k + 1]).then_inc(xhi_made, 1)

            def keep_k(row):
                act.wait_ge(qk_done, row.over(1) * 4 + KH)
                if later(row - 1):
                    act.wait_ge(s_done, (row - 1).counts())
                for m in range(KH):
                    act.activation(k_sb[:, m], ps_qk[:, KH + m], ACT.Identity,
                                   bias=b_in[:, KH + m:KH + m + 1]).then_inc(qk_kept, 1)

            def keep_q(row):
                act.wait_ge(qk_done, row.counts(4))
                for m in range(KH):
                    for h in range(2):
                        lanes = slice(D * h, D * (h + 1))
                        act.activation(q_sb[lanes, m, :, h], ps_qk[lanes, m].rearrange("p (a b) -> p a b", b=QB),
                                       ACT.Identity, bias=bq[lanes, m:m + 1], scale=QSCALE).then_inc(qk_kept, 1)

            def keep_v(row):
                half = row.slot(2)
                act.wait_ge(v_done, row.counts())
                if later(row - 2):
                    act.wait_ge(o_done, (row - 2).counts())
                    act.wait_ge(v_moved[half], (row.over(2)) * 48)
                act.activation(v_even[:, half, :, :, 0:D],
                               ps_v[:].rearrange("p t (h d) -> p t h d", h=HEADS), ACT.Identity).then_inc(v_kept, 1)

            def exponent(row):
                act.wait_ge(s_shifted, row.counts())
                if later(row - 1):
                    act.wait_ge(p_turned, (row - 1).counts())
                act.activation(prob[:], score[:].rearrange("p a b -> p (a b)"), ACT.Exp).then_inc(exp_done, 1)

            def keep_p(row):
                act.wait_ge(p_turned, row.counts())
                if later(row - 1):
                    act.wait_ge(o_done, (row - 1).counts())
                for c in range(2):
                    lanes = slice(KB * c, KB * (c + 1))
                    act.activation(probT[lanes, :, :, c], ps_p[lanes].rearrange("p i (h q) -> p i h q", q=QB),
                                   ACT.Identity).then_inc(p_kept, 1)

            def o_high(row):
                act.wait_ge(o_turned, row.counts())
                if later(row - 1):
                    act.wait_ge(y_done, (row - 1).counts())
                for k in range(KH):
                    act.activation(oT[:, 0, k, 0:SEQ], ps_oT[:, k], ACT.Identity,
                                   bias=b_in[:, 2 * KH + k:2 * KH + k + 1]).then_inc(ohi_made, 1)

            act.wait_ge(consts_in, 16 * CONSTS)
            act.wait_ge(zeros_set, 2)
            act.activation(bq[:], b_in[:, 0:KH], ACT.Identity, scale=QSCALE).then_inc(bq_made, 1)
            act.wait_ge(bq_made, 1)
            for k in range(KH):
                act.activation(wo_hi[:, k], w_out[:, k], ACT.Identity).then_inc(fin_act, 1)
            split_w(0)
            x_high(Row(0), 0)
            keep_k(Row(0))
            keep_q(Row(0))
            keep_v(Row(0))
            x_high(Row(1), 0)

            def step(t, b, pair):
                if later(t - 1):
                    o_high(t - 1)
                if exists(t + 1):
                    keep_k(t + 1)
                exponent(t)
                if exists(t + 1):
                    keep_q(t + 1)
                if t.turn is None and t.fixed == LOOP0_END:
                    split_w(1)
                keep_p(t)
                if exists(t + 2):
                    x_high(t + 2, batch_of(t + 2, b))
                if exists(t + 1):
                    keep_v(t + 1)

            main(act, step)
            o_high(Row(ROWS - 1))

        @block.gpsimd
        def _(pool):
            pool.memset(v_even[:, :, :, :, D:E], 1.0).then_inc(ones_set, 1)
            pool.memset(q_sb[:], 0.0).then_inc(zeros_set, 1)
            pool.memset(probT[:], 0.0).then_inc(zeros_set, 1)
            pool.wait_ge(consts_in, 16 * CONSTS)

            def residual(row):
                pool.wait_ge(x_in[row.slot(XRING) // 2], (row.over(XRING) + 1) * 16)
                at = row.slot(XRING)
                if later(row - XRING):
                    pool.wait_ge(y_out[at], row.over(XRING) * 16)
                pool.tensor_tensor(res[:, at], xr[:, at], b_out[:].unsqueeze(1).broadcast_to([P, TT, C]),
                                   ALU.add).then_inc(res_made, 1)

            def halo(row):
                pool.wait_ge(olo_made, row.counts(KH))
                stand_alone(pool, pool_idle, row)
                pool.tensor_copy(oT[:, :, :, SEQ:SEQ + HALO], oT[:, :, :, 0:HALO]).then_inc(halo_made, 1)

            def wrap_x(row):
                pool.wait_ge(xlo_made, row.counts(KH))
                stand_alone(pool, pool_idle, row)
                h = row.slot(2)
                pool.tensor_copy(xT[:, h, :, :, 0:HALO], xT[:, h, :, :, SEQ:SEQ + HALO]).then_inc(x_wrapped, 1)

            residual(Row(0))
            wrap_x(Row(0))
            residual(Row(1))

            def step(t, b, pair):
                if exists(t + 1):
                    wrap_x(t + 1)
                if later(t - 1):
                    halo(t - 1)
                if exists(t + 2):
                    residual(t + 2)

            main(pool, step)
            halo(Row(ROWS - 1))

        @block.vector
        def _(dve):
            def take_stats(bank, k, pair_no):
                return dve.bn_stats(moments[:, k, bass.ds(pair_no, 1)].rearrange("p a s -> p (a s)"), bank)

            with dve.Fori(0, FIRST_CHUNKS // STAT_RING) as turn:
                for n in range(STAT_RING):
                    for bank in range(4):
                        k, u = bank // 2, bank % 2
                        dve.wait_ge(stat_turned, turn * (4 * STAT_RING) + 4 * n + bank + 1)
                        take_stats(stat_banks[bank], k, turn * (2 * STAT_RING) + 2 * n + u).then_inc(stat_taken, 1)

            def finish_stats(b):
                count = [FD * b]

                def then(ins):
                    count[0] += 1
                    ins.then_inc(fin_dve, 1)
                    dve.wait_ge(fin_dve, count[0])

                pairs = ROWS // 2 // B
                for k in range(KH):
                    then(dve.bn_aggr(stat[:, k], moments[:, k, pairs * b:pairs * (b + 1)]
                                     .rearrange("p a s -> p (a s)")))
                dve.wait_ge(fin_pe, 2 * b + 1)
                g = ps_x_flat[:, 0:2 * KH].rearrange("p (a b) -> p a b", b=2)
                then(dve.tensor_scalar(neg_mean[b][:], g[:, :, 0], -1.0, None, ALU.mult))
                then(dve.tensor_tensor(t1[:], stat[:, :, 0], neg_mean[b][:], ALU.add))
                then(dve.tensor_tensor(t2[:], t1[:], t1[:], ALU.mult))
                dve.wait_ge(fin_pe, 2 * b + 2)
                then(dve.tensor_scalar(t1[:], g[:, :, 1], EPS, None, ALU.add))
                then(dve.tensor_tensor(t1[:], ps_x_flat[:, 8:8 + KH], t1[:], ALU.add))
                dve.wait_ge(fin_act, KH + (KH + 1) * b + 1)
                then(dve.reciprocal(rstd[:], rstd[:]))
                then(dve.tensor_tensor(t2[:], rstd[:], rstd[:], ALU.mult))
                then(dve.tensor_tensor(t2[:], t2[:], t1[:], ALU.mult))
                then(dve.tensor_scalar(t2[:], t2[:], -0.5, 1.5, ALU.mult, ALU.add))
                then(dve.tensor_tensor(rstd[:], rstd[:], t2[:], ALU.mult))
                for k in range(KH):
                    then(dve.tensor_scalar(w_scaled[:, k], w_in[:, k], rstd[:, k:k + 1], None, ALU.mult))
                for k in range(KH):
                    dve.wait_ge(fin_act, KH + (KH + 1) * b + k + 2)
                    then(dve.tensor_tensor(w_lo[b][:, k], w_scaled[:, k], w_hi[b][:, k].bitcast(F32), ALU.subtract))

            def x_low(row, b):
                dve.wait_ge(xhi_made, row.counts(KH))
                for k in range(KH):
                    dve.scalar_tensor_tensor(out=xT[:, row.slot(2), 1, k, HALO:], in0=ps_x[:, k],
                                             scalar=neg_mean[b][:, k:k + 1],
                                             in1=xT[:, row.slot(2), 0, k, HALO:].bitcast(F32),
                                             op0=ALU.add, op1=ALU.subtract).then_inc(xlo_made, 1)

            def mask_scores(row):
                dve.wait_ge(s_done, row.counts())
                if later(row - 1):
                    dve.wait_ge(exp_done, (row - 1).counts())
                dve.tensor_tensor(score[:], ps_s[:], mask[:].rearrange("p (a b) -> p a b", b=KB),
                                  ALU.add).then_inc(s_masked, 1)

            def shift_scores(row):
                dve.wait_ge(s_masked, row.counts())
                dve.tensor_reduce(peak[:], score[:], AX_X, ALU.max).then_inc(peak_found, 1)
                dve.wait_ge(peak_found, row.counts())
                dve.tensor_tensor(score[:], score[:], peak[:].unsqueeze(2).broadcast_to([P, NB, KB]),
                                  ALU.subtract).then_inc(s_shifted, 1)

            def o_low(row):
                dve.wait_ge(ohi_made, row.counts(KH))
                for k in range(KH):
                    dve.scalar_tensor_tensor(out=oT[:, 1, k, 0:SEQ], in0=ps_oT[:, k],
                                             scalar=b_in[:, 2 * KH + k:2 * KH + k + 1],
                                             in1=oT[:, 0, k, 0:SEQ].bitcast(F32),
                                             op0=ALU.add, op1=ALU.subtract).then_inc(olo_made, 1)

            def keep_y(row):
                dve.wait_ge(y_done, row.counts())
                dve.wait_ge(res_made, row.counts())
                at = row.slot(XRING)
                dve.tensor_tensor(res[:, at], ps_y, res[:, at], ALU.add).then_inc(y_kept, 1)

            def keep_o(row):
                dve.wait_ge(o_done, row.counts())
                o = ps_o[:, :, 0:HEADS * E].rearrange("p t (h e) -> p t h e", e=E)
                dve.reciprocal(inv[:], o[:, :, :, D]).then_inc(inv_made, 1)
                dve.wait_ge(inv_made, row.counts())
                if later(row - 1):
                    dve.wait_ge(o_turned, (row - 1).counts())
                dve.tensor_tensor(o_sb[:].rearrange("p t (h d) -> p t h d", h=HEADS), o[:, :, :, 0:D],
                                  inv[:].unsqueeze(3).broadcast_to([P, TT, HEADS, D]),
                                  ALU.mult).then_inc(o_kept, 1)

            dve.wait_ge(consts_in, 16 * CONSTS)
            for k in range(KH):
                dve.wait_ge(fin_act, k + 1)
                dve.tensor_tensor(wo_lo[:, k], w_out[:, k], wo_hi[:, k].bitcast(F32), ALU.subtract)
            finish_stats(0)
            x_low(Row(0), 0)
            x_low(Row(1), 0)

            def step(t, b, pair):
                mask_scores(t)
                if later(t - 1):
                    o_low(t - 1)
                shift_scores(t)
                if pair is not None:
                    dve.wait_ge(pair_turned, pair.counts())
                    take_stats(ps_x_flat, pair.slot(2), pair.over(2) + (R + CHUNK) // 2).then_inc(pair_taken, 1)
                if t.turn is None and t.fixed == LOOP0_END:
                    finish_stats(1)
                if later(t - 1):
                    keep_y(t - 1)
                if exists(t + 2):
                    x_low(t + 2, batch_of(t + 2, b))
                keep_o(t)

            main(dve, step)
            o_low(Row(ROWS - 1))
            keep_y(Row(ROWS - 1))


def kernel(**inputs):
    import concourse.bacc as bacc
    from concourse.bass_utils import run_bass_kernel_spmd

    x = np.ascontiguousarray(inputs["x"])
    b_in, b_out = np.asarray(inputs["L0_conv_b_in"]), np.asarray(inputs["L0_conv_b_out"])
    mask, unit, average = constants(x.shape[2])
    arrays = {
        "x": x,
        "w_in_t": np.ascontiguousarray(np.asarray(inputs["L0_conv_w_in"]).T),
        "w_out_t": np.ascontiguousarray(np.asarray(inputs["L0_conv_w_out"]).T),
        "b_in_c": np.ascontiguousarray(b_in.reshape(-1, P).T),
        "b_out_r": np.ascontiguousarray(np.broadcast_to(b_out, (P, b_out.size))),
        "mask": mask, "unit": unit, "average": average,
    }
    nc = bacc.Bacc("TRN2", target_bir_lowering=False, num_devices=1)
    args = [nc.dram_tensor(f"in_{n}", a.shape, mybir.dt.from_np(a.dtype), kind="ExternalInput").ap()
            for n, a in arrays.items()]
    out = nc.dram_tensor("out", x.shape, F32, kind="ExternalOutput").ap()
    banded_attention(nc, *args, out)
    r = run_bass_kernel_spmd(nc, [{f"in_{n}": a for n, a in arrays.items()}], core_ids=[0])
    return r.results[0]["out"]
```

```python
from contextlib import ExitStack

import numpy as np

import concourse.bass as bass
from concourse import mybir
from concourse.alu_op_type import AluOpType as ALU

F32 = mybir.dt.float32
F32R = mybir.dt.float32r
ACT = mybir.ActivationFunctionType
AX_X = mybir.AxisListType.X

P = 128
HEADS = 4
BAND = 16
GROUPS = 32
EPS = 1e-5
MASKED = -1e30
QB = 32
KB = 64
XRING = 4
STAT_RING = 4
CHUNK = 4


def block_order(seq):
    wide = seq // KB
    even = [(KB * a + BAND, KB * a, 2 * a + 1) for a in range(wide)]
    odd = [((KB * a - BAND) % seq, (KB * a - QB) % seq, 2 * a) for a in range(wide)]
    return even + odd


def constants(seq):
    mask = np.full((P, seq // QB, KB), MASKED, np.float32)
    for blk, (q0, k0, _) in enumerate(block_order(seq)):
        q = (q0 + np.arange(QB)) % seq
        k = (k0 + np.arange(KB)) % seq
        keep = np.abs(q[:, None] - k[None, :]) <= BAND
        mask[:, blk][np.tile(keep, (HEADS, 1))] = 0.0
    unit = np.eye(P, dtype=np.float32)
    size = 2 * P // GROUPS
    average = np.kron(np.eye(P // size, dtype=np.float32), np.full((size, size), 1.0 / size, np.float32))
    spread = np.kron(np.eye(GROUPS, dtype=np.float32), np.ones((1, size), np.float32))
    return mask.reshape(P, -1), unit, average, spread


class Row:

    def __init__(self, fixed, turn=None):
        self.fixed, self.turn = fixed, turn

    def __add__(self, n):
        return Row(self.fixed + n, self.turn)

    def __sub__(self, n):
        return self + -n

    def over(self, n):
        if self.turn is None:
            return self.fixed // n
        return self.turn * (XRING // n) + self.fixed // n

    def slot(self, n):
        return self.fixed % n

    def counts(self, per_row=1):
        return (self.over(1) + 1) * per_row


def banded_attention(nc, x, w_in_t, w_out_t, b_in_c, b_out_r, mask_d, unit_d, average_d, spread_d, out):
    B, R, SEQ, C = x.shape
    D = C // HEADS
    KH = C // P
    TT = SEQ // P
    NB = SEQ // QB
    W3 = 3 * C
    ROWS = B * R
    QSCALE = float(D) ** -0.5
    assert (B, HEADS * QB, KH, TT, D, KB) == (2, P, 2, 2, 64, 2 * QB) and 2 * BAND == QB
    HALO = BAND
    BLOCKS = block_order(SEQ)

    GS = C // GROUPS
    LEAD = CHUNK
    LOOP0, LOOP0_END = 2, R - 6
    LOOP1, LOOP1_END = R, ROWS - XRING
    SUMS = R - LEAD
    assert (LOOP0_END - LOOP0) % XRING == 0 and (LOOP1_END - LOOP1) % XRING == 0
    assert LOOP0_END <= SUMS and CHUNK == XRING == 4 and R % (CHUNK * STAT_RING) == 0

    x_rows = x.rearrange("b r (t p) c -> p (b r) t c", p=P)
    out_rows = out.rearrange("b r (t p) c -> p (b r) t c", p=P)

    with ExitStack() as ctx:
        def sb(name, shape, dt=F32):
            return ctx.enter_context(nc.sbuf_tensor(name, shape, dt))

        def psum(name, shape):
            return ctx.enter_context(nc.psum_tensor(name, shape, F32))

        def sem(name):
            return ctx.enter_context(nc.semaphore(name))

        unit = sb("unit", [P, P])
        average = sb("average", [P, P])
        spread = sb("spread", [GROUPS, C])
        lanes_mean = sb("lanes_mean", [P, P])
        mask = sb("mask", [P, NB * KB])
        b_in = sb("b_in", [P, W3 // P])
        bq = sb("bq", [P, KH])
        b_out = sb("b_out", [P, C])
        w_in = sb("w_in", [P, KH, W3])
        w_out = sb("w_out", [P, KH, C])
        w_scaled = sb("w_scaled", [P, KH, W3])
        w_hi = [sb(f"w_hi{b}", [P, KH, W3], F32R) for b in range(B)]
        w_lo = [sb(f"w_lo{b}", [P, KH, W3], F32R) for b in range(B)]
        wo_hi = sb("wo_hi", [P, KH, C], F32R)
        wo_lo = sb("wo_lo", [P, KH, C], F32R)

        stat_x = sb("stat_x", [P, STAT_RING, CHUNK * TT, C])
        moments = sb("moments", [P, KH, R // 2, 6])
        nat_x = sb("nat_x", [P, KH, CHUNK * TT, P])
        nat_moments = sb("nat_moments", [P, GROUPS, R // CHUNK, 6])
        nat_sum = sb("nat_sum", [P, 3, GROUPS])
        nat_mean = sb("nat_mean", [P, GROUPS])
        nat_off = sb("nat_off", [P, GROUPS, 2 * R // CHUNK])
        nat_cols = sb("nat_cols", [GROUPS, 2])
        stat = sb("stat", [P, KH, 2])
        neg_mean = [sb(f"neg_mean{b}", [P, KH]) for b in range(B)]
        rstd = sb("rstd", [P, KH])
        t1 = sb("t1", [P, KH])
        t2 = sb("t2", [P, KH])

        xr = sb("xr", [P, XRING, TT, C])
        res = sb("res", [P, XRING, TT, C])
        xT = sb("xT", [P, 2, 2, KH, HALO + SEQ], F32R)
        q_sb = sb("q_sb", [P, KH, NB, 2, QB])
        k_sb = sb("k_sb", [P, KH, SEQ])
        v_even = sb("v_even", [P, 2, TT, C])
        v_odd = sb("v_odd", [P, 2, TT, C])
        score = sb("score", [P, NB, KB])
        peak = sb("peak", [P, NB])
        prob = sb("prob", [P, NB * KB])
        probT = sb("probT", [P, 4, HEADS, 2, QB])
        total = sb("total", [P, NB])
        oT = sb("oT", [P, 2, KH, SEQ + HALO], F32R)

        ps_x = psum("ps_x", [P, KH, SEQ])
        ps_qk = psum("ps_qk", [P, 4, SEQ])
        ps_v = psum("ps_v", [P, TT, C])
        ps_s = psum("ps_s", [P, NB, KB])
        ps_p = psum("ps_p", [P, 4, P])
        ps_o = psum("ps_o", [P, KH, SEQ])
        ps_y = psum("ps_y", [P, TT, C])
        stat_banks = [ps_x[:].rearrange("p a b -> p (a b)"), ps_v[:].rearrange("p a b -> p (a b)"),
                      ps_qk[:, 0:2].rearrange("p a b -> p (a b)"), ps_qk[:, 2:4].rearrange("p a b -> p (a b)")]
        ps_x_flat = stat_banks[0]

        consts_in = sem("consts_in")
        stat_in = [sem(f"stat_in{i}") for i in range(STAT_RING)]
        stat_turned = sem("stat_turned")
        stat_taken = sem("stat_taken")
        nat_in = [sem(f"nat_in{i}") for i in range(KH)]
        nat_taken = sem("nat_taken")
        fin_dve = sem("fin_dve")
        fin_pe = sem("fin_pe")
        fin_act = sem("fin_act")
        zeros_set = sem("zeros_set")
        bq_made = sem("bq_made")
        pe_idle = sem("pe_idle")
        pool_idle = sem("pool_idle")

        x_in = [sem(f"x_in{i}") for i in range(2)]
        x_turned = sem("x_turned")
        xhi_made = sem("xhi_made")
        xlo_made = sem("xlo_made")
        res_made = sem("res_made")
        qk_done = sem("qk_done")
        qk_kept = sem("qk_kept")
        x_wrapped = sem("x_wrapped")
        v_done = sem("v_done")
        v_kept = sem("v_kept")
        v_moved = [sem(f"v_moved{i}") for i in range(2)]
        s_done = sem("s_done")
        s_masked = sem("s_masked")
        peak_found = sem("peak_found")
        s_shifted = sem("s_shifted")
        exp_done = sem("exp_done")
        total_made = sem("total_made")
        total_inverted = sem("total_inverted")
        p_made = sem("p_made")
        p_turned = sem("p_turned")
        p_kept = sem("p_kept")
        o_done = sem("o_done")
        ohi_made = sem("ohi_made")
        olo_made = sem("olo_made")
        halo_made = sem("halo_made")
        y_done = sem("y_done")
        y_kept = sem("y_kept")
        y_out = [sem(f"y_out{i}") for i in range(XRING)]

        CONSTS = 8
        MEANS, VARIANCES, DEVIATIONS, WEIGHTS = (3, 26), (7, 27), (12, 32), (16, 36)
        QK_STEPS = 3 * KH

        block = ctx.enter_context(nc.Block())

        def main(eng, step):
            def quarter(t):
                return t + LEAD if t.turn is not None or t.fixed < SUMS else None

            for t in range(LOOP0):
                step(Row(t), 0, quarter(Row(t)))
            with eng.Fori(0, (LOOP0_END - LOOP0) // XRING) as turn:
                for k in range(XRING):
                    t = Row(LOOP0 + k, turn)
                    step(t, 0, quarter(t))
            for t in range(LOOP0_END, R):
                step(Row(t), 0, quarter(Row(t)))
            with eng.Fori(0, (LOOP1_END - LOOP1) // XRING) as turn:
                for k in range(XRING):
                    step(Row(LOOP1 + k, turn), 1, None)
            for t in range(LOOP1_END, ROWS):
                step(Row(t), 1, None)

        def at_step(t, n):
            return t.turn is None and t.fixed == n

        def stand_alone(eng, idle, row):
            if row.turn is not None:
                eng.sem_inc(idle, 1)

        def exists(row):
            return row.turn is not None or 0 <= row.fixed < ROWS

        def batch_of(row, b):
            return row.fixed // R if row.turn is None else b

        def later(row):
            return row.turn is not None or row.fixed >= 0

        @block.sync
        def _(sp):
            for dst, src in ((unit, unit_d), (average, average_d), (mask, mask_d), (b_in, b_in_c),
                             (b_out, b_out_r), (spread, spread_d)):
                sp.dma_start(dst[:], src).then_inc(consts_in, 16)
            sp.dma_start(w_in[:], w_in_t.rearrange("(k p) n -> p k n", p=P)).then_inc(consts_in, 16)
            sp.dma_start(w_out[:], w_out_t.rearrange("(k p) n -> p k n", p=P)).then_inc(consts_in, 16)

            def load_stat(place, turn_no, wait):
                if wait is not None:
                    sp.wait_ge(stat_turned, wait)
                sp.dma_start(stat_x[:, place].rearrange("p (r t) c -> p r t c", t=TT),
                             x_rows[:, bass.ds(turn_no * CHUNK, CHUNK)]).then_inc(stat_in[place], 16)

            for n in range(STAT_RING):
                load_stat(n, n, None)
            with sp.Fori(0, R // CHUNK // STAT_RING - 1) as turn:
                for n in range(STAT_RING):
                    load_stat(n, turn * STAT_RING + STAT_RING + n, turn * (4 * STAT_RING) + 4 * (n + 1))

            def load_x(row):
                if row.turn is not None or row.fixed >= XRING:
                    sp.wait_ge(x_turned, (row - XRING + 1).counts())
                    sp.wait_ge(res_made, (row - XRING + 1).counts())
                at = row.slot(XRING)
                sp.dma_start(xr[:, at:at + 2], x_rows[:, bass.ds(row.over(1), 2)]).then_inc(
                    x_in[row.slot(XRING) // 2], 16)

            def load_nat(chunk, k):
                sp.dma_start(nat_x[:, k].rearrange("p (r t) c -> p r t c", t=TT),
                             x_rows[:, bass.ds(chunk * -CHUNK + (ROWS - CHUNK), CHUNK), :, P * k:P * (k + 1)]
                             ).then_inc(nat_in[k], 16)

            def next_nat(quarter):
                if quarter.slot(2) == 1 and (quarter.turn is not None or quarter.fixed + CHUNK < R):
                    sp.wait_ge(nat_taken, quarter.counts())
                    load_nat(quarter.over(CHUNK) + 1, quarter.slot(CHUNK) // 2)

            load_x(Row(0))
            load_x(Row(2))
            for k in range(KH):
                load_nat(0, k)
            for n in range(LEAD):
                next_nat(Row(n))

            def step(t, b, quarter):
                if t.fixed % 2 == 0 and exists(t + XRING):
                    load_x(t + XRING)
                if exists(t - 1):
                    store(t - 1)
                if exists(t + 1):
                    move_v(t + 1)
                if quarter is not None:
                    next_nat(quarter)

            def store(row):
                sp.wait_ge(y_kept, row.counts())
                at = row.slot(XRING)
                sp.dma_start(out_rows[:, bass.ds(row.over(1), 1)], res[:, at:at + 1]).then_inc(y_out[at], 16)

            def move_v(row):
                sp.wait_ge(v_kept, row.counts())
                if later(row - 2):
                    sp.wait_ge(o_done, (row - 2).counts())
                h = row.slot(2)
                sp.dma_start(v_odd[QB:P, h], v_even[0:P - QB, h]).then_inc(v_moved[h], 16)
                sp.dma_start(v_odd[0:QB, h, 0], v_even[P - QB:P, h, TT - 1]).then_inc(v_moved[h], 16)
                sp.dma_start(v_odd[0:QB, h, 1], v_even[P - QB:P, h, 0]).then_inc(v_moved[h], 16)

            move_v(Row(0))
            main(sp, step)
            store(Row(ROWS - 1))
            for at in range(XRING):
                sp.wait_ge(y_out[at], 16 * (ROWS // XRING))

        @block.tensor
        def _(pe):
            def mm(o, l, r, start=True, stop=True):
                return pe.matmul(o, l, r, start=start, stop=stop)

            pe.wait_ge(consts_in, 16 * CONSTS)

            def turn_chunk(n, before):
                for bank in range(4):
                    k, u = bank // 2, bank % 2
                    if before is not None:
                        pe.wait_ge(stat_taken, before - 4 + bank + 1)
                    for j in range(4):
                        last = pe.transpose(stat_banks[bank][:, P * j:P * (j + 1)],
                                            stat_x[:, n, 4 * u + j, P * k:P * (k + 1)], unit[:])
                    last.then_inc(stat_turned, 1)

            for n in range(STAT_RING):
                pe.wait_ge(stat_in[n], 16)
                turn_chunk(n, 4 * n if n else None)
            with pe.Fori(0, R // CHUNK // STAT_RING - 1) as turn:
                for n in range(STAT_RING):
                    pe.wait_ge(stat_in[n], turn * 16 + 32)
                    turn_chunk(n, turn * (4 * STAT_RING) + 4 * (STAT_RING + n))

            def average_groups():
                pe.wait_ge(fin_dve, 2)
                mm(ps_x_flat[:, 0:2 * KH], average[:], stat[:].rearrange("p a b -> p (a b)")).then_inc(fin_pe, 1)
                pe.wait_ge(fin_dve, 5)
                mm(ps_x_flat[:, 8:8 + KH], average[:], t2[:]).then_inc(fin_pe, 1)

            def average_lanes(t):
                if at_step(t, SUMS + 1):
                    pe.wait_ge(fin_dve, 17)
                    mm(ps_x_flat[:, 0:GROUPS], lanes_mean[:], nat_sum[:, 0])
                    mm(ps_x_flat[0:GROUPS, 64:65], nat_sum[:, 0], lanes_mean[:, 0:1]).then_inc(fin_pe, 1)
                if at_step(t, SUMS + 2):
                    pe.wait_ge(fin_dve, 24)
                    mm(ps_x_flat[0:GROUPS, 0:1], nat_sum[:, 1], lanes_mean[:, 0:1]).then_inc(fin_pe, 1)
                    pe.wait_ge(fin_dve, 25)
                    for k in range(KH):
                        last = mm(ps_x_flat[:, 8 + 2 * k:10 + 2 * k], spread[:, P * k:P * (k + 1)], nat_cols[:])
                    last.then_inc(fin_pe, 1)

            def turn_x(row):
                pe.wait_ge(x_in[row.slot(XRING) // 2], (row.over(XRING) + 1) * 16)
                if later(row - 1):
                    pe.wait_ge(xlo_made, (row - 1).counts(KH))
                if at_step(row, 0):
                    pe.wait_ge(fin_dve, VARIANCES[0])
                if at_step(row, SUMS + 3):
                    pe.wait_ge(fin_dve, 20)
                if at_step(row, R):
                    pe.wait_ge(fin_dve, VARIANCES[1])
                for k in range(KH):
                    for t in range(TT):
                        last = pe.transpose(ps_x[:, k, P * t:P * (t + 1)],
                                            xr[:, row.slot(XRING), t, P * k:P * (k + 1)], unit[:])
                last.then_inc(x_turned, 1)

            def three(o, l_hi, l_lo, r_hi, r_lo, k):
                mm(o, l_hi, r_hi, start=k == 0, stop=False)
                mm(o, l_hi, r_lo, start=False, stop=False)
                return mm(o, l_lo, r_hi, start=False, stop=k == KH - 1)

            def project_k(row, b):
                if row.turn is None and row.fixed % R == 0:
                    pe.wait_ge(fin_dve, WEIGHTS[b])
                pe.wait_ge(xlo_made, row.counts(KH))
                if later(row - 1):
                    pe.wait_ge(qk_kept, (row - 1).over(1) * QK_STEPS + KH)
                turned_product(row, b, (KH, KH + 1), slice(HALO, HALO + SEQ))

            def project_q(row, b):
                pe.wait_ge(x_wrapped, row.counts())
                if later(row - 1):
                    pe.wait_ge(qk_kept, (row - 1).counts(QK_STEPS))
                turned_product(row, b, range(KH), slice(0, SEQ))

            def turned_product(row, b, parts, tokens):
                h = row.slot(2)
                for m in parts:
                    cols = slice(P * m, P * (m + 1))
                    for k in range(KH):
                        last = three(ps_qk[:, m], w_hi[b][:, k, cols], w_lo[b][:, k, cols],
                                     xT[:, h, 0, k, tokens], xT[:, h, 1, k, tokens], k)
                    last.then_inc(qk_done, 1)

            def project_v(row, b):
                h = row.slot(2)
                if later(row - 1):
                    pe.wait_ge(v_kept, (row - 1).counts())
                for t in range(TT):
                    cols = slice(HALO + P * t, HALO + P * (t + 1))
                    for k in range(KH):
                        last = three(ps_v[:, t], xT[:, h, 0, k, cols], xT[:, h, 1, k, cols],
                                     w_hi[b][:, k, 2 * C:], w_lo[b][:, k, 2 * C:], k)
                last.then_inc(v_done, 1)

            def window(ap, start, size):
                if start + size <= SEQ:
                    return ap[:, start:start + size]
                n = SEQ - start
                assert n * 2 == size
                return ap.rearrange("p (a b) -> p a b", b=n)[:, ::-(SEQ // n - 1)]

            def scores(row):
                pe.wait_ge(qk_kept, row.counts(QK_STEPS))
                if later(row - 1):
                    pe.wait_ge(s_masked, (row - 1).counts())
                stand_alone(pe, pe_idle, row)
                for blk, (_, k0, place) in enumerate(BLOCKS):
                    for two in range(KH):
                        last = mm(ps_s[2 * QB * two:2 * QB * (two + 1), blk],
                                  q_sb[:, two, place].rearrange("p a b -> p (a b)"),
                                  window(k_sb[:, two], k0, KB))
                last.then_inc(s_done, 1)

            def turn_p(row):
                pe.wait_ge(p_made, row.counts())
                if later(row - 1):
                    pe.wait_ge(p_kept, (row - 1).counts(2))
                for i in range(4):
                    last = pe.transpose(ps_p[:, i], prob[:, P * i:P * (i + 1)], unit[:])
                last.then_inc(p_turned, 1)

            def weigh_v(row):
                half = row.slot(2)
                pe.wait_ge(p_kept, row.counts(2))
                pe.wait_ge(v_moved[half], (row.over(2) + 1) * 48)
                if later(row - 1):
                    pe.wait_ge(olo_made, (row - 1).counts(KH))
                stand_alone(pe, pe_idle, row)
                for i in range(4):
                    v, odd = (v_even, 1) if i < 2 else (v_odd, 0)
                    pair = slice(2 * (i % 2), 2 * (i % 2) + 2)
                    for h in range(HEADS):
                        o = ps_o[D * (h % 2):D * (h % 2 + 1), h // 2].rearrange("p (a u q) -> p a u q", u=2, q=QB)
                        last = mm(o[:, pair, odd], v[:, half, i % 2, D * h:D * (h + 1)], probT[:, i, h])
                last.then_inc(o_done, 1)

            def project_out(row):
                pe.wait_ge(halo_made, row.counts())
                if later(row - 1):
                    pe.wait_ge(y_kept, (row - 1).counts())
                for t in range(TT):
                    cols = slice(HALO + P * t, HALO + P * (t + 1))
                    for k in range(KH):
                        last = three(ps_y[:, t], oT[:, 0, k, cols], oT[:, 1, k, cols],
                                     wo_hi[:, k], wo_lo[:, k], k)
                last.then_inc(y_done, 1)

            average_groups()
            turn_x(Row(0))
            project_k(Row(0), 0)
            project_q(Row(0), 0)
            project_v(Row(0), 0)
            turn_x(Row(1))

            def step(t, b, quarter):
                scores(t)
                if exists(t + 1):
                    project_k(t + 1, batch_of(t + 1, b))
                if later(t - 1):
                    weigh_v(t - 1)
                if exists(t + 1):
                    project_q(t + 1, batch_of(t + 1, b))
                average_lanes(t)
                if exists(t + 2):
                    turn_x(t + 2)
                if exists(t + 1):
                    project_v(t + 1, batch_of(t + 1, b))
                if later(t - 1):
                    project_out(t - 1)
                turn_p(t)

            main(pe, step)
            weigh_v(Row(ROWS - 1))
            project_out(Row(ROWS - 1))

        @block.scalar
        def _(act):
            def split_w(b):
                act.wait_ge(fin_dve, VARIANCES[b])
                act.activation(rstd[:], t1[:], ACT.Sqrt).then_inc(fin_act, 1)
                for k in range(KH):
                    act.wait_ge(fin_dve, DEVIATIONS[b] + 1 + k)
                    act.activation(w_hi[b][:, k], w_scaled[:, k], ACT.Identity).then_inc(fin_act, 1)

            def x_high(row, b):
                if row.turn is None and row.fixed % R == 0:
                    act.wait_ge(fin_dve, MEANS[b])
                act.wait_ge(x_turned, row.counts())
                if later(row - 2):
                    act.wait_ge(v_done, (row - 2).counts())
                for k in range(KH):
                    act.activation(xT[:, row.slot(2), 0, k, HALO:], ps_x[:, k], ACT.Identity,
                                   bias=neg_mean[b][:, k:k + 1]).then_inc(xhi_made, 1)

            def keep_k(row):
                act.wait_ge(qk_done, row.over(1) * 4 + KH)
                if later(row - 1):
                    act.wait_ge(s_done, (row - 1).counts())
                for m in range(KH):
                    act.activation(k_sb[:, m], ps_qk[:, KH + m], ACT.Identity,
                                   bias=b_in[:, KH + m:KH + m + 1]).then_inc(qk_kept, 1)

            def keep_q(row, m):
                act.wait_ge(qk_done, row.counts(4))
                for h in range(2):
                    lanes = slice(D * h, D * (h + 1))
                    act.activation(q_sb[lanes, m, :, h], ps_qk[lanes, m].rearrange("p (a b) -> p a b", b=QB),
                                   ACT.Identity, bias=bq[lanes, m:m + 1], scale=QSCALE).then_inc(qk_kept, 1)

            def keep_v(row):
                half = row.slot(2)
                act.wait_ge(v_done, row.counts())
                if later(row - 2):
                    act.wait_ge(o_done, (row - 2).counts())
                    act.wait_ge(v_moved[half], (row.over(2)) * 48)
                act.activation(v_even[:, half], ps_v[:], ACT.Identity).then_inc(v_kept, 1)

            def exponent(row):
                act.wait_ge(s_shifted, row.counts())
                if later(row - 1):
                    act.wait_ge(p_turned, (row - 1).counts())
                act.activation(prob[:], score[:].rearrange("p a b -> p (a b)"), ACT.Exp).then_inc(exp_done, 1)

            def keep_p(row):
                act.wait_ge(p_turned, row.counts())
                if later(row - 1):
                    act.wait_ge(o_done, (row - 1).counts())
                for c in range(2):
                    lanes = slice(KB * c, KB * (c + 1))
                    act.activation(probT[lanes, :, :, c], ps_p[lanes].rearrange("p i (h q) -> p i h q", q=QB),
                                   ACT.Identity).then_inc(p_kept, 1)

            def o_high(row):
                act.wait_ge(o_done, row.counts())
                if later(row - 1):
                    act.wait_ge(y_done, (row - 1).counts())
                for k in range(KH):
                    act.activation(oT[:, 0, k, 0:SEQ], ps_o[:, k], ACT.Identity,
                                   bias=b_in[:, 2 * KH + k:2 * KH + k + 1]).then_inc(ohi_made, 1)

            act.wait_ge(consts_in, 16 * CONSTS)
            act.wait_ge(zeros_set, 3)
            act.activation(bq[:], b_in[:, 0:KH], ACT.Identity, scale=QSCALE).then_inc(bq_made, 1)
            act.wait_ge(bq_made, 1)
            for k in range(KH):
                act.activation(wo_hi[:, k], w_out[:, k], ACT.Identity).then_inc(fin_act, 1)
            split_w(0)
            x_high(Row(0), 0)
            keep_k(Row(0))
            for m in range(KH):
                keep_q(Row(0), m)
            keep_v(Row(0))
            x_high(Row(1), 0)

            def step(t, b, quarter):
                if exists(t + 1):
                    keep_k(t + 1)
                exponent(t)
                if later(t - 1):
                    o_high(t - 1)
                if exists(t + 1):
                    keep_q(t + 1, 0)
                if exists(t + 2):
                    x_high(t + 2, batch_of(t + 2, b))
                if exists(t + 1):
                    keep_q(t + 1, 1)
                    keep_v(t + 1)
                keep_p(t)
                if at_step(t, SUMS + 2):
                    split_w(1)

            main(act, step)
            o_high(Row(ROWS - 1))

        @block.gpsimd
        def _(pool):
            pool.memset(lanes_mean[:], 1.0 / (P * 2 * R // CHUNK)).then_inc(zeros_set, 1)
            pool.memset(q_sb[:], 0.0).then_inc(zeros_set, 1)
            pool.memset(probT[:], 0.0).then_inc(zeros_set, 1)
            pool.wait_ge(consts_in, 16 * CONSTS)

            def residual(row):
                pool.wait_ge(x_in[row.slot(XRING) // 2], (row.over(XRING) + 1) * 16)
                at = row.slot(XRING)
                if later(row - XRING):
                    pool.wait_ge(y_out[at], row.over(XRING) * 16)
                pool.tensor_tensor(res[:, at], xr[:, at], b_out[:].unsqueeze(1).broadcast_to([P, TT, C]),
                                   ALU.add).then_inc(res_made, 1)

            def halo(row):
                pool.wait_ge(olo_made, row.counts(KH))
                stand_alone(pool, pool_idle, row)
                pool.tensor_copy(oT[:, :, :, SEQ:SEQ + HALO], oT[:, :, :, 0:HALO]).then_inc(halo_made, 1)

            def wrap_x(row):
                pool.wait_ge(xlo_made, row.counts(KH))
                stand_alone(pool, pool_idle, row)
                h = row.slot(2)
                pool.tensor_copy(xT[:, h, :, :, 0:HALO], xT[:, h, :, :, SEQ:SEQ + HALO]).then_inc(x_wrapped, 1)

            residual(Row(0))
            wrap_x(Row(0))
            residual(Row(1))

            def step(t, b, quarter):
                if exists(t + 1):
                    wrap_x(t + 1)
                if later(t - 1):
                    halo(t - 1)
                if exists(t + 2):
                    residual(t + 2)

            main(pool, step)
            halo(Row(ROWS - 1))

        @block.vector
        def _(dve):
            def take_stats(bank, k, pair_no):
                return dve.bn_stats(moments[:, k, bass.ds(pair_no, 1)].rearrange("p a s -> p (a s)"), bank)

            with dve.Fori(0, R // CHUNK // STAT_RING) as turn:
                for n in range(STAT_RING):
                    for bank in range(4):
                        k, u = bank // 2, bank % 2
                        dve.wait_ge(stat_turned, turn * (4 * STAT_RING) + 4 * n + bank + 1)
                        take_stats(stat_banks[bank], k, turn * (2 * STAT_RING) + 2 * n + u).then_inc(stat_taken, 1)

            def take_quarter(quarter):
                n = quarter.slot(CHUNK)
                dve.wait_ge(nat_in[n // 2], (quarter.over(CHUNK) + 1) * 16)
                for j in range(GROUPS // 4):
                    at = (GROUPS // 4 * (n % 2) + j) * GS
                    last = dve.bn_stats(nat_moments[:, GROUPS // 4 * n + j, bass.ds(quarter.over(CHUNK), 1)]
                                        .rearrange("p a s -> p (a s)"), nat_x[:, n // 2, :, at:at + GS])
                last.then_inc(nat_taken, 1)

            def then(count, ins):
                ins.then_inc(fin_dve, 1)
                dve.wait_ge(fin_dve, count)

            def sum_nat(t):
                seen = nat_moments[:].rearrange("p g c (e s) -> p g (c e) s", e=2)
                means, squares = seen[:, :, :, 1], seen[:, :, :, 2]
                if at_step(t, SUMS):
                    dve.wait_ge(nat_taken, R)
                    then(17, dve.tensor_reduce(nat_sum[:, 0], means, AX_X, ALU.add))
                    then(18, dve.tensor_reduce(nat_sum[:, 1], squares, AX_X, ALU.add))
                if at_step(t, SUMS + 1):
                    dve.wait_ge(fin_pe, 3)
                    then(19, dve.tensor_copy(nat_mean[:], ps_x_flat[:, 0:GROUPS]))
                    then(20, dve.tensor_copy(nat_cols[:, 0:1], ps_x_flat[0:GROUPS, 64:65]))
                if at_step(t, SUMS + 2):
                    part = CHUNK * TT * GS // 2
                    then(23, dve.tensor_reduce(nat_sum[:, 2], nat_off[:], AX_X, ALU.add))
                    then(24, dve.scalar_tensor_tensor(out=nat_sum[:, 1], in0=nat_sum[:, 2], scalar=float(part),
                                                      in1=nat_sum[:, 1], op0=ALU.mult, op1=ALU.add))
                    dve.wait_ge(fin_pe, 4)
                    then(25, dve.tensor_copy(nat_cols[:, 1:2], ps_x_flat[0:GROUPS, 0:1]))
                    dve.wait_ge(fin_pe, 5)
                    both = ps_x_flat[:, 8:8 + 2 * KH].rearrange("p (k a) -> p k a", a=2)
                    then(26, dve.tensor_scalar(neg_mean[1][:], both[:, :, 0], -1.0, None, ALU.mult))
                    then(27, dve.tensor_scalar(t1[:], both[:, :, 1], 1.0 / part, EPS, ALU.mult, ALU.add))

            def square_nat(t):
                if at_step(t, SUMS + 1):
                    means = nat_moments[:].rearrange("p g c (e s) -> p g (c e) s", e=2)[:, :, :, 1]
                    then(21, dve.tensor_tensor(nat_off[:], means, nat_mean[:].unsqueeze(2).broadcast_to(
                        [P, GROUPS, 2 * R // CHUNK]), ALU.subtract))
                    then(22, dve.tensor_tensor(nat_off[:], nat_off[:], nat_off[:], ALU.mult))

            def finish_turned():
                dve.wait_ge(stat_taken, 4 * (R // CHUNK))
                for k in range(KH):
                    then(1 + k, dve.bn_aggr(stat[:, k], moments[:, k].rearrange("p a s -> p (a s)")))
                dve.wait_ge(fin_pe, 1)
                g = ps_x_flat[:, 0:2 * KH].rearrange("p (a b) -> p a b", b=2)
                then(3, dve.tensor_scalar(neg_mean[0][:], g[:, :, 0], -1.0, None, ALU.mult))
                then(4, dve.tensor_tensor(t1[:], stat[:, :, 0], neg_mean[0][:], ALU.add))
                then(5, dve.tensor_tensor(t2[:], t1[:], t1[:], ALU.mult))
                dve.wait_ge(fin_pe, 2)
                then(6, dve.tensor_scalar(t1[:], g[:, :, 1], EPS, None, ALU.add))
                then(7, dve.tensor_tensor(t1[:], ps_x_flat[:, 8:8 + KH], t1[:], ALU.add))

            def scale_weights(b):
                n = VARIANCES[b]
                dve.wait_ge(fin_act, KH + (KH + 1) * b + 1)
                then(n + 1, dve.reciprocal(rstd[:], rstd[:]))
                then(n + 2, dve.tensor_tensor(t2[:], rstd[:], rstd[:], ALU.mult))
                then(n + 3, dve.tensor_tensor(t2[:], t2[:], t1[:], ALU.mult))
                then(n + 4, dve.tensor_scalar(t2[:], t2[:], -0.5, 1.5, ALU.mult, ALU.add))
                then(n + 5, dve.tensor_tensor(rstd[:], rstd[:], t2[:], ALU.mult))
                n = DEVIATIONS[b]
                for k in range(KH):
                    then(n + 1 + k, dve.tensor_scalar(w_scaled[:, k], w_in[:, k], rstd[:, k:k + 1], None, ALU.mult))
                for k in range(KH):
                    dve.wait_ge(fin_act, KH + (KH + 1) * b + k + 2)
                    then(n + 3 + k, dve.tensor_tensor(w_lo[b][:, k], w_scaled[:, k], w_hi[b][:, k].bitcast(F32),
                                                      ALU.subtract))

            def x_low(row, b):
                dve.wait_ge(xhi_made, row.counts(KH))
                for k in range(KH):
                    dve.scalar_tensor_tensor(out=xT[:, row.slot(2), 1, k, HALO:], in0=ps_x[:, k],
                                             scalar=neg_mean[b][:, k:k + 1],
                                             in1=xT[:, row.slot(2), 0, k, HALO:].bitcast(F32),
                                             op0=ALU.add, op1=ALU.subtract).then_inc(xlo_made, 1)

            def mask_scores(row):
                dve.wait_ge(s_done, row.counts())
                if later(row - 1):
                    dve.wait_ge(exp_done, (row - 1).counts())
                dve.tensor_tensor(score[:], ps_s[:], mask[:].rearrange("p (a b) -> p a b", b=KB),
                                  ALU.add).then_inc(s_masked, 1)

            def find_peaks(row):
                dve.wait_ge(s_masked, row.counts())
                dve.tensor_reduce(peak[:], score[:], AX_X, ALU.max).then_inc(peak_found, 1)

            def shift_scores(row):
                dve.wait_ge(peak_found, row.counts())
                dve.tensor_tensor(score[:], score[:], peak[:].unsqueeze(2).broadcast_to([P, NB, KB]),
                                  ALU.subtract).then_inc(s_shifted, 1)

            def o_low(row):
                dve.wait_ge(ohi_made, row.counts(KH))
                for k in range(KH):
                    dve.scalar_tensor_tensor(out=oT[:, 1, k, 0:SEQ], in0=ps_o[:, k],
                                             scalar=b_in[:, 2 * KH + k:2 * KH + k + 1],
                                             in1=oT[:, 0, k, 0:SEQ].bitcast(F32),
                                             op0=ALU.add, op1=ALU.subtract).then_inc(olo_made, 1)

            def keep_y(row):
                dve.wait_ge(y_done, row.counts())
                dve.wait_ge(res_made, row.counts())
                at = row.slot(XRING)
                dve.tensor_tensor(res[:, at], ps_y[:], res[:, at], ALU.add).then_inc(y_kept, 1)

            def sum_exps(row):
                dve.wait_ge(exp_done, row.counts())
                dve.tensor_reduce(total[:], prob[:].rearrange("p (a b) -> p a b", b=KB), AX_X,
                                  ALU.add).then_inc(total_made, 1)
                dve.wait_ge(total_made, row.counts())
                dve.reciprocal(total[:], total[:]).then_inc(total_inverted, 1)

            def divide_exps(row):
                dve.wait_ge(total_inverted, row.counts())
                p = prob[:].rearrange("p (a b) -> p a b", b=KB)
                dve.tensor_tensor(p, p, total[:].unsqueeze(2).broadcast_to([P, NB, KB]),
                                  ALU.mult).then_inc(p_made, 1)

            dve.wait_ge(consts_in, 16 * CONSTS)
            for k in range(KH):
                dve.wait_ge(fin_act, k + 1)
                dve.tensor_tensor(wo_lo[:, k], w_out[:, k], wo_hi[:, k].bitcast(F32), ALU.subtract)
            finish_turned()
            scale_weights(0)
            x_low(Row(0), 0)
            for n in range(LEAD):
                take_quarter(Row(n))
            x_low(Row(1), 0)

            def step(t, b, quarter):
                mask_scores(t)
                find_peaks(t)
                shift_scores(t)
                sum_exps(t)
                if later(t - 1):
                    o_low(t - 1)
                divide_exps(t)
                sum_nat(t)
                if exists(t + 2):
                    x_low(t + 2, batch_of(t + 2, b))
                if quarter is not None:
                    take_quarter(quarter)
                if later(t - 1):
                    keep_y(t - 1)
                square_nat(t)
                if at_step(t, SUMS + 2):
                    scale_weights(1)

            main(dve, step)
            o_low(Row(ROWS - 1))
            keep_y(Row(ROWS - 1))


def kernel(**inputs):
    import concourse.bacc as bacc
    from concourse.bass_utils import run_bass_kernel_spmd

    x = np.ascontiguousarray(inputs["x"])
    b_in, b_out = np.asarray(inputs["L0_conv_b_in"]), np.asarray(inputs["L0_conv_b_out"])
    mask, unit, average, spread = constants(x.shape[2])
    arrays = {
        "x": x,
        "w_in_t": np.ascontiguousarray(np.asarray(inputs["L0_conv_w_in"]).T),
        "w_out_t": np.ascontiguousarray(np.asarray(inputs["L0_conv_w_out"]).T),
        "b_in_c": np.ascontiguousarray(b_in.reshape(-1, P).T),
        "b_out_r": np.ascontiguousarray(np.broadcast_to(b_out, (P, b_out.size))),
        "mask": mask, "unit": unit, "average": average, "spread": spread,
    }
    nc = bacc.Bacc("TRN2", target_bir_lowering=False, num_devices=1)
    args = [nc.dram_tensor(f"in_{n}", a.shape, mybir.dt.from_np(a.dtype), kind="ExternalInput").ap()
            for n, a in arrays.items()]
    out = nc.dram_tensor("out", x.shape, F32, kind="ExternalOutput").ap()
    banded_attention(nc, *args, out)
    r = run_bass_kernel_spmd(nc, [{f"in_{n}": a for n, a in arrays.items()}], core_ids=[0])
    return r.results[0]["out"]
```
